# Optimizing a Trainium2 kernel written in Bass

```python
import numpy as np
import jax
import jax.numpy as jnp

def _softmax(x, axis=-1):
    return jax.nn.softmax(x, axis=axis)

def _gelu(x):
    return jax.nn.gelu(x, approximate=True)

def _silu(x):
    return jax.nn.silu(x)

def _sigmoid(x):
    return jax.nn.sigmoid(x)

def _layernorm(x, axis=-1, eps=1e-05):
    m = jnp.mean(x, axis=axis, keepdims=True)
    v = jnp.var(x, axis=axis, keepdims=True)
    return (x - m) / jnp.sqrt(v + eps)

def _scatter_add(tgt, idx, src, axis=0):
    return tgt.at[idx].add(src)

def _segment_sum(src, seg, n):
    return jax.ops.segment_sum(src, seg, n)
kernel_name = 'mk_cond_resid_d1_seqx_r4_2e2794'

def setup_inputs(seed: int=0):
    np.random.seed(seed)
    _w = jnp.asarray

    def _rec_inputs():
        import jax
        import jax.numpy as jnp
        _rk = jax.random.key(seed)
        x = 8.748e-05 + 1 * jax.random.normal(jax.random.fold_in(_rk, 1), (16, 256, 512), jnp.float32)
        _lenS = 256 - jax.random.randint(jax.random.fold_in(_rk, 7), (16,), 0, max(1, 256 // 4) + 1, jnp.int32)
        _lenS2 = 256 - jax.random.randint(jax.random.fold_in(_rk, 8), (16,), 0, max(1, 256 // 4) + 1, jnp.int32)
        cond_2048 = -9.80646e-05 + 1.00041 * jax.random.normal(jax.random.fold_in(_rk, 11), (16, 512), jnp.float32)
        return (x, cond_2048)
    x, cond_2048 = _rec_inputs()

    def _L0_cond_setup():
        import jax, jax.numpy as jnp
        import numpy as np
        DT = 0.01
        EPSILON = 0.08
        ALPHA = 0.7
        BETA = 0.8
        CLAMP = 20.0
        B, T, N = (64, 128, 512)

        def _derivative(q, p, drive, coupling, bias):
            i_couple = jnp.tanh(q) @ coupling.T
            dq = q - q ** 3 / 3.0 - p + drive + i_couple + bias
            dp = EPSILON * (q + ALPHA - BETA * p)
            return (dq, dp)

        def _rk4_step(q, p, drive, coupling, bias):
            dq1, dp1 = _derivative(q, p, drive, coupling, bias)
            dq2, dp2 = _derivative(q + 0.5 * DT * dq1, p + 0.5 * DT * dp1, drive, coupling, bias)
            dq3, dp3 = _derivative(q + 0.5 * DT * dq2, p + 0.5 * DT * dp2, drive, coupling, bias)
            dq4, dp4 = _derivative(q + DT * dq3, p + DT * dp3, drive, coupling, bias)
            q_next = q + DT / 6.0 * (dq1 + 2 * dq2 + 2 * dq3 + dq4)
            p_next = p + DT / 6.0 * (dp1 + 2 * dp2 + 2 * dp3 + dp4)
            q_next = jnp.clip(q_next, -CLAMP, CLAMP)
            p_next = jnp.clip(p_next, -CLAMP, CLAMP)
            return (q_next, p_next)
        key = jax.random.key(seed)
        k1, k2, k3, k4 = jax.random.split(key, 4)
        return {'q0': jax.random.normal(k1, (B, N), dtype=jnp.float32), 'p0': jax.random.normal(k2, (B, N), dtype=jnp.float32), 'input_drive_seq': jax.random.normal(k3, (B, T, N), dtype=jnp.float32), 'coupling': jax.random.normal(k4, (N, N), dtype=jnp.float32) * 0.01, 'bias': jnp.zeros((N,), dtype=jnp.float32)}
    _L0_cond_all = _L0_cond_setup()
    _L0_cond_in = {k: v for k, v in _L0_cond_all.items() if k in ('coupling', 'bias')}
    del _L0_cond_all
    return {'x': x, 'cond_2048': cond_2048, 'L0_cond_coupling': _L0_cond_in['coupling'], 'L0_cond_bias': _L0_cond_in['bias']}

def reference(x, cond_2048, L0_cond_coupling, L0_cond_bias):
    import jax
    import jax.numpy as jnp

    def _L0_cond_ref(q0, p0, input_drive_seq, coupling, bias):
        import jax, jax.numpy as jnp
        import numpy as np
        DT = 0.01
        EPSILON = 0.08
        ALPHA = 0.7
        BETA = 0.8
        CLAMP = 20.0
        B, T, N = (64, 128, 512)

        def _derivative(q, p, drive, coupling, bias):
            i_couple = jnp.tanh(q) @ coupling.T
            dq = q - q ** 3 / 3.0 - p + drive + i_couple + bias
            dp = EPSILON * (q + ALPHA - BETA * p)
            return (dq, dp)

        def _rk4_step(q, p, drive, coupling, bias):
            dq1, dp1 = _derivative(q, p, drive, coupling, bias)
            dq2, dp2 = _derivative(q + 0.5 * DT * dq1, p + 0.5 * DT * dp1, drive, coupling, bias)
            dq3, dp3 = _derivative(q + 0.5 * DT * dq2, p + 0.5 * DT * dp2, drive, coupling, bias)
            dq4, dp4 = _derivative(q + DT * dq3, p + DT * dp3, drive, coupling, bias)
            q_next = q + DT / 6.0 * (dq1 + 2 * dq2 + 2 * dq3 + dq4)
            p_next = p + DT / 6.0 * (dp1 + 2 * dp2 + 2 * dp3 + dp4)
            q_next = jnp.clip(q_next, -CLAMP, CLAMP)
            p_next = jnp.clip(p_next, -CLAMP, CLAMP)
            return (q_next, p_next)
        drive_tbn = jnp.swapaxes(input_drive_seq, 0, 1)

        def scan_fn(carry, drive):
            q, p = carry
            q, p = _rk4_step(q, p, drive, coupling, bias)
            return ((q, p), q)
        (_, _), q_trace_tbn = jax.lax.scan(scan_fn, (q0, p0), drive_tbn)
        return jnp.swapaxes(q_trace_tbn, 0, 1)
    x = x + _L0_cond_ref(cond_2048, cond_2048, x, L0_cond_coupling, L0_cond_bias)
    return x

_drawn_inputs = setup_inputs


def setup_inputs(seed=0):
    import zlib

    import numpy as np

    out = dict(_drawn_inputs(seed))
    spreads = {'L0_cond_bias': (0.0, 0.1)}
    factors = {}
    for name, (base, spread) in spreads.items():
        noise = np.random.default_rng([zlib.crc32(name.encode()), seed]).standard_normal(out[name].shape)
        drawn = base * np.exp(spread * noise) if base else spread * noise
        out[name] = jnp.asarray(drawn.astype(out[name].dtype))
    for name, factor in factors.items():
        out[name] = (out[name] * factor).astype(out[name].dtype)
    return out
```

```python
import concourse.bass as bass
from concourse import mybir
from contextlib import ExitStack


fp32 = mybir.dt.float32
fp16 = mybir.dt.float16
u32 = mybir.dt.uint32
ALU = mybir.AluOpType
ACT = mybir.ActivationFunctionType
AX = mybir.AxisListType

DT, EPSILON, ALPHA, BETA, CLAMP = 0.01, 0.08, 0.7, 0.8, 20.0
LO = 2048.0
STEP_H = [0.5 * DT, 0.5 * DT, DT, DT / 6]
SCALE_OF = [0, 0, 1, 2]
H3 = [0.5 * DT, DT, DT / 6]


def build(nc, x, cond, coupling, bias, out):
    B, T, N = x.shape
    P = 128
    J = N // P
    F = J * B
    K = 4
    CH = 4
    NCH = T // CH
    ROWS = B * CH
    SG = K * CH

    x_chunks = x.rearrange("b (c t) n -> c b t n", t=CH)
    out_chunks = out.rearrange("b (c t) (h jj n) -> c jj b t h n", t=CH, jj=2, n=P)

    ctx = ExitStack()
    with ctx:
        def sb(name, shape, dt=fp32):
            return ctx.enter_context(nc.sbuf_tensor(name, shape, dt))

        def pb(name, shape):
            return ctx.enter_context(nc.psum_tensor(name, shape, fp32))

        def sem(name):
            return ctx.enter_context(nc.semaphore(name))

        ident = sb("ident", [P, P])
        c_nat = sb("c_nat", [P, J, N])
        w_scaled = sb("w_scaled", [P, N])
        w_rest = sb("w_rest", [P, N])
        w_hi = sb("w_hi", [P, J, N], fp16)
        w_lo = sb("w_lo", [P, J, N], fp16)
        c_top = sb("c_top", [P, 4])
        inv_s = sb("inv_s", [P, 1])
        s_up = sb("s_up", [P, 1])
        g_hi_scale = sb("g_hi_scale", [P, 3])
        g_lo_scale = sb("g_lo_scale", [P, 3])
        cond_nat = sb("cond_nat", [B, N])
        bias_nat = sb("bias_nat", [J, P])
        bias3 = sb("bias3", [P, 3, F])

        x_nat = sb("x_nat", [ROWS, N])
        x_t = sb("x_t", [P, CH, F])
        x3 = sb("x3", [P, 3, F])
        drive3 = sb("drive3", [P, 3, F])
        y_t = sb("y_t", [P, F * CH])
        y_nat = sb("y_nat", [P, J // 2, P])

        q_in = sb("q_in", [P, K, F])
        q0 = sb("q0", [P, F])
        p_in = sb("p_in", [P, K, F])
        p_new = sb("p_new", [P, F])
        t_hilo = sb("t_hilo", [P, J, 2, B], fp16)
        t_full = sb("t_full", [P, F])
        t_hi_up = sb("t_hi_up", [P, F], fp16)
        q_sq = sb("q_sq", [P, F])
        cubic = sb("cubic", [P, F])
        q_drive3 = sb("q_drive3", [P, 3, F])
        base = sb("base", [P, K, F])
        pre = sb("pre", [P, K, F])
        part = sb("part", [P, F])
        leak = sb("leak", [P, K, F])
        alpha2 = sb("alpha2", [P, 2, F])
        p_off = sb("p_off", [P, 2, F])
        base_last = sb("base_last", [P, F])
        dq = sb("dq", [P, 3, F])
        dq_twice = sb("dq_twice", [P, F])
        dq_sum2 = sb("dq_sum2", [P, F])
        dq_sum = sb("dq_sum", [P, F])
        leak_twice = sb("leak_twice", [P, 2, F])
        leak_sum = sb("leak_sum", [P, 3, F])

        wt_ps = [pb("wt_ps0", [P, N]), pb("wt_ps1", [P, N])]
        g_ps = pb("g_ps", [P, J, 2, B])
        x_ps = pb("x_ps", [P, F * CH])
        y_ps = pb("y_ps", [P, J // 2, P])
        setup_ps = pb("setup_ps", [P, F + J])

        ident_zeroed, ident_ready = sem("ident_zeroed"), sem("ident_ready")
        coupling_in, cond_in, bias_in = sem("coupling_in"), sem("cond_in"), sem("bias_in")
        top_of_rows, top_of_all, setup_chain = sem("top_of_rows"), sem("top_of_all"), sem("setup_chain")
        weights_turned, weights_taken = sem("weights_turned"), sem("weights_taken")
        setup_turned, bias_ready, p_start = sem("setup_turned"), sem("bias_ready"), sem("p_start")
        x_in, x_turned = sem("x_in"), sem("x_turned")
        y_turned, y_out_ready, y_stored = sem("y_turned"), sem("y_out_ready"), sem("y_stored")
        x_next, drive_ready, q_clipped, p_clipped = sem("x_next"), sem("drive_ready"), sem("q_clipped"), sem("p_clipped")
        p_off_ready, y_done, pool_prev = sem("p_off_ready"), sem("y_done"), sem("pool_prev")
        sums_ready, dq_doubled, leak_doubled, leak_sum_a = (sem("sums_ready"), sem("dq_doubled"), sem("leak_doubled"), sem("leak_sum_a"))
        drives_added, step_sum, p_summed = sem("drives_added"), sem("step_sum"), sem("p_summed")
        q_ready, leak_ready, th_hi, th_full = sem("q_ready"), sem("leak_ready"), sem("th_hi"), sem("th_full")
        th_hi_up, th_lo, sq_ready, cubic_ready = sem("th_hi_up"), sem("th_lo"), sem("sq_ready"), sem("cubic_ready")
        pre_ready, coupled, part_ready = sem("pre_ready"), sem("coupled"), sem("part_ready")

        def over_chunks(eng, body):
            body(0, True, False)
            with eng.Fori(1, NCH - 1) as i:
                body(i, False, False)
            body(NCH - 1, False, True)

        block = ctx.enter_context(nc.Block())

        @block.sync
        def _(sp):
            sp.dma_start(c_nat[:, :, :], coupling.rearrange("(j p) m -> p j m", p=P)).then_inc(coupling_in, 16)
            sp.dma_start(cond_nat[:, :], cond).then_inc(cond_in, 16)
            sp.dma_start(bias_nat[:, :], bias.rearrange("(j p) -> j p", p=P)).then_inc(bias_in, 16)
            sp.dma_start(x_nat[:, :], x_chunks[0]).then_inc(x_in, 16)

            def chunk(i, first, last):
                if not last:
                    sp.wait_ge(x_turned, i + 1)
                if not first:
                    store(i - 1)
                    sp.wait_ge(y_stored, 32 * i)
                if not last:
                    sp.dma_start(x_nat[:, :], x_chunks[i + 1]).then_inc(x_in, 16)

            def store(c):
                sp.wait_ge(y_out_ready, c + 1)
                for jj in range(2):
                    sp.dma_start(out_chunks[c, jj], y_nat[jj * ROWS:(jj + 1) * ROWS, :, :]).then_inc(y_stored, 16)

            over_chunks(sp, chunk)
            store(NCH - 1)
            sp.wait_ge(y_stored, 32 * NCH)

        @block.tensor
        def _(pe):
            pe.wait_ge(ident_ready, 1)
            pe.wait_ge(cond_in, 16)
            for j in range(J):
                pe.transpose(setup_ps[:, j * B:(j + 1) * B], cond_nat[:, j * P:(j + 1) * P], ident[0:B, 0:B])
            pe.wait_ge(bias_in, 16)
            pe.transpose(setup_ps[:, F:F + J], bias_nat[:, :], ident[0:J, 0:J]).then_inc(setup_turned, 1)
            pe.wait_ge(coupling_in, 16)
            for k in range(J):
                if k >= 2:
                    pe.wait_ge(weights_taken, k - 1)
                for j in range(J):
                    last = pe.transpose(wt_ps[k % 2][:, j * P:(j + 1) * P], c_nat[:, j, k * P:(k + 1) * P], ident[:, :])
                last.then_inc(weights_turned, 1)

            def turn_x(c):
                for j in range(J):
                    last = pe.transpose(x_ps[:, j * ROWS:(j + 1) * ROWS], x_nat[:, j * P:(j + 1) * P],
                                        ident[0:ROWS, 0:ROWS])
                last.then_inc(x_turned, 1)

            def turn_y(c):
                pe.wait_ge(y_done, CH * (c + 1))
                for h in range(J // 2):
                    last = pe.transpose(y_ps[:, h, :], y_t[:, h * P:(h + 1) * P], ident[:, :])
                last.then_inc(y_turned, 1)

            pe.wait_ge(x_in, 16)
            turn_x(0)
            pe.wait_ge(weights_taken, J)

            def couple(n):
                pe.wait_ge(th_hi, n + 1)
                for j in range(J):
                    for k in range(J):
                        pe.matmul(g_ps[:, j, 1, :], w_lo[:, k, j * P:(j + 1) * P], t_hilo[:, k, 0, :],
                                  start=(j == 0 and k == 0), stop=False, skip_group_check=True)
                pe.wait_ge(th_lo, n + 1)
                for j in range(J):
                    for k in range(J):
                        last = pe.matmul(g_ps[:, j, :, :], w_hi[:, k, j * P:(j + 1) * P], t_hilo[:, k, :, :],
                                         start=False, stop=(j == J - 1 and k == J - 1), skip_group_check=True)
                last.then_inc(coupled, 1)

            def chunk(i, first, last):
                for s in range(CH):
                    for k in range(K):
                        if s == CH - 1 and k == 0 and not last:
                            pe.wait_ge(x_in, 16 * (i + 2))
                        couple(SG * i + K * s + k)
                        if s == 0 and k == 2 and not first:
                            turn_y(i - 1)
                        if s == CH - 1 and k == 0 and not last:
                            turn_x(i + 1)

            over_chunks(pe, chunk)
            turn_y(NCH - 1)

        @block.scalar
        def _(act):
            act.preload_act_table(ACT.Tanh)

            def take_x(step, s):
                src = x_ps[:, s:F * CH:CH]
                act.copy(x_t[:, s, :], src)
                for m in range(3):
                    last = act.mul(x3[:, m, :], src, H3[m])
                last.then_inc(x_next, 1)

            act.wait_ge(x_turned, 1)
            take_x(0, 0)

            def tanh_parts(n, k, step):
                act.wait_ge(q_ready, n + 1)
                q = q_in[:, k, :].rearrange("p (j b) -> p j b", j=J)
                act.activation(t_hilo[:, :, 0, :], q, ACT.Tanh).then_inc(th_hi, 1)
                act.activation(t_full[:, :], q_in[:, k, :], ACT.Tanh).then_inc(th_full, 1)
                if k == 0:
                    act.wait_ge(q_clipped, step + 1)
                act.activation(q_sq[:, :], q0[:, :] if k == 0 else q_in[:, k, :], ACT.Square).then_inc(sq_ready, 1)

            def chunk(i, first, last):
                for s in range(CH):
                    for k in range(K):
                        step = CH * i + s
                        tanh_parts(SG * i + K * s + k, k, step)
                        if k == 2 and not (last and s == CH - 1):
                            act.wait_ge(drive_ready, step + 1)
                            if s == CH - 1:
                                act.wait_ge(x_turned, i + 2)
                            take_x(step + 1, (s + 1) % CH)
                        if s == 0 and k == 3 and not first:
                            take_y(i - 1)

            def take_y(c):
                act.wait_ge(y_turned, c + 1)
                act.copy(y_nat[:, :, :], y_ps[:, :, :]).then_inc(y_out_ready, 1)

            over_chunks(act, chunk)
            act.wait_ge(y_stored, 32 * (NCH - 1))
            take_y(NCH - 1)

        @block.gpsimd
        def _(pool):
            nc.gpsimd.memset(ident[:, :], 0.0).then_inc(ident_zeroed, 1)
            pool.wait_ge(ident_zeroed, 1)
            nc.gpsimd.affine_select(out=ident[:, :], in_=ident[:, :], compare_op=ALU.not_equal, fill=1.0, base=0,
                                    pattern=[[-1, P]], channel_multiplier=1).then_inc(ident_ready, 1)
            pool.wait_ge(top_of_rows, 1)
            nc.gpsimd.partition_all_reduce(c_top[:, 3:4], c_top[:, 2:3], P, bass.bass_isa.ReduceOp.max).then_inc(top_of_all, 1)
            pool.wait_ge(bias_ready, 1)

            def add_bias(step):
                pool.wait_ge(x_next, step + 1)
                pool.tensor_tensor(drive3[:, :, :], x3[:, :, :], bias3[:, :, :], ALU.add).then_inc(drive_ready, 1)

            add_bias(0)

            def finish_step(step, s):
                pool.wait_ge(q_clipped, step + 2)
                pool.tensor_tensor(y_t[:, s:F * CH:CH], q0[:, :], x_t[:, s, :], ALU.add).then_inc(y_done, 1)

            def chunk(i, first, last):
                for s in range(CH):
                    step = CH * i + s
                    n = SG * i + K * s
                    pool.wait_ge(p_clipped, step + 1)
                    pool.tensor_tensor(p_off[:, :, :], p_in[:, 0, :].unsqueeze(1).broadcast_to([P, 2, F]),
                                       alpha2[:, :, :], ALU.add).then_inc(p_off_ready, 1)
                    if not (first and s == 0):
                        finish_step(step - 1, (s - 1) % CH)
                    pool.wait_ge(leak_ready, n + 2)
                    pool.tensor_tensor(dq[:, 0, :], q_in[:, 1, :], q0[:, :], ALU.subtract)
                    pool.tensor_tensor(leak_twice[:, 0, :], leak[:, 1, :], leak[:, 1, :], ALU.add).then_inc(leak_doubled, 1)
                    pool.wait_ge(leak_doubled, 2 * step + 1)
                    pool.tensor_tensor(leak_sum[:, 0, :], leak_twice[:, 0, :], leak[:, 0, :], ALU.add).then_inc(leak_sum_a, 1)
                    pool.wait_ge(leak_ready, n + 3)
                    pool.tensor_tensor(dq[:, 1, :], q_in[:, 2, :], q0[:, :], ALU.subtract).then_inc(dq_doubled, 1)
                    pool.tensor_tensor(leak_twice[:, 1, :], leak[:, 2, :], leak[:, 2, :], ALU.add).then_inc(leak_doubled, 1)
                    pool.wait_ge(dq_doubled, 2 * step + 1)
                    pool.tensor_tensor(dq_twice[:, :], dq[:, 1, :], dq[:, 1, :], ALU.add).then_inc(dq_doubled, 1)
                    pool.wait_ge(leak_doubled, 2 * step + 2)
                    pool.tensor_tensor(leak_sum[:, 1, :], leak_twice[:, 1, :], leak_sum[:, 0, :], ALU.add)
                    pool.wait_ge(dq_doubled, 2 * step + 2)
                    pool.tensor_tensor(dq_sum2[:, :], dq_twice[:, :], dq[:, 0, :], ALU.add).then_inc(sums_ready, 1)
                    if not (last and s == CH - 1):
                        add_bias(step + 1)

            over_chunks(pool, chunk)
            finish_step(T - 1, CH - 1)

        @block.vector
        def _(dve):
            links = [0]

            def link(ins):
                links[0] += 1
                ins.then_inc(setup_chain, 1)
                dve.wait_ge(setup_chain, links[0])

            dve.wait_ge(coupling_in, 16)
            link(dve.tensor_reduce(c_top[:, 0:1], c_nat[:, :, :], AX.XY, ALU.max))
            link(dve.tensor_reduce(c_top[:, 1:2], c_nat[:, :, :], AX.XY, ALU.min))
            dve.scalar_tensor_tensor(c_top[:, 2:3], c_top[:, 1:2], -1.0, c_top[:, 0:1], ALU.mult,
                                     ALU.max).then_inc(top_of_rows, 1)
            dve.wait_ge(top_of_all, 1)
            link(dve.tensor_scalar(inv_s[:, :], c_top[:, 3:4], 2.0 ** -100, None, ALU.max))
            link(dve.tensor_scalar(s_up[:, :].bitcast(u32), inv_s[:, :].bitcast(u32), 0x7F800000, None, ALU.bitwise_and))
            link(dve.tensor_scalar(inv_s[:, :], s_up[:, :], 2.0 ** -14, None, ALU.mult))
            link(dve.reciprocal(s_up[:, :], inv_s[:, :]))
            for m in range(3):
                link(dve.tensor_scalar(g_hi_scale[:, m:m + 1], inv_s[:, :], H3[m], None, ALU.mult))
                link(dve.tensor_scalar(g_lo_scale[:, m:m + 1], inv_s[:, :], H3[m] / LO, None, ALU.mult))
            dve.wait_ge(setup_turned, 1)
            for m in range(3):
                bias_cols = setup_ps[:, F:F + J].unsqueeze(2).broadcast_to([P, J, B])
                link(dve.tensor_scalar(bias3[:, m, :].rearrange("p (j b) -> p j b", j=J), bias_cols, H3[m], None, ALU.mult))
            for m in range(2):
                link(dve.memset(alpha2[:, m, :], H3[m] * EPSILON * ALPHA))
            dve.tensor_copy(p_in[:, 0, :], setup_ps[:, 0:F]).then_inc(p_clipped, 1)
            dve.tensor_copy(q_in[:, 0, :], setup_ps[:, 0:F]).then_inc(bias_ready, 1)
            for k in range(J):
                dve.wait_ge(weights_turned, k + 1)
                link(dve.tensor_scalar(w_scaled[:, :], wt_ps[k % 2][:, :], s_up[:, 0:1], None, ALU.mult))
                link(dve.tensor_copy(w_hi[:, k, :], w_scaled[:, :]))
                link(dve.scalar_tensor_tensor(w_rest[:, :], w_hi[:, k, :], -1.0, w_scaled[:, :], ALU.mult, ALU.add))
                dve.tensor_scalar(w_lo[:, k, :], w_rest[:, :], LO, None, ALU.mult).then_inc(weights_taken, 1)
                dve.wait_ge(weights_taken, k + 1)
            dve.sem_inc(q_ready, 1)

            def clip_q(n):
                dve.wait_ge(q_ready, n + 1)
                dve.tensor_scalar(q0[:, :], q_in[:, 0, :], CLAMP, -CLAMP, ALU.min, ALU.max).then_inc(q_clipped, 1)

            def split_tanh(n):
                dve.wait_ge(th_hi, n + 1)
                dve.tensor_scalar(t_hi_up[:, :].rearrange("p (j b) -> p j b", j=J), t_hilo[:, :, 0, :], LO, None,
                                  ALU.mult).then_inc(th_hi_up, 1)
                dve.wait_ge(th_hi_up, n + 1)
                dve.wait_ge(th_full, n + 1)
                dve.scalar_tensor_tensor(t_hilo[:, :, 1, :], t_full[:, :].rearrange("p (j b) -> p j b", j=J), LO,
                                         t_hi_up[:, :].rearrange("p (j b) -> p j b", j=J), ALU.mult,
                                         ALU.subtract).then_inc(th_lo, 1)

            def take_cubic(n, q):
                dve.wait_ge(sq_ready, n + 1)
                dve.scalar_tensor_tensor(cubic[:, :], q_sq[:, :], -3.0, q, ALU.add, ALU.mult).then_inc(cubic_ready, 1)

            def take_pre(k, base_k):
                return dve.scalar_tensor_tensor(pre[:, k, :], cubic[:, :], -STEP_H[k] / 3.0, base_k, ALU.mult, ALU.add)

            def take_leak(n, k, q):
                return dve.scalar_tensor_tensor(leak[:, k, :], p_in[:, k, :], -BETA, q, ALU.mult, ALU.add).then_inc(leak_ready, 1)

            def next_p(k):
                return dve.scalar_tensor_tensor(p_in[:, k + 1, :], leak[:, k, :], STEP_H[k] * EPSILON,
                                                p_off[:, SCALE_OF[k], :], ALU.mult, ALU.add)

            def less_p(out_, k, m):
                return dve.scalar_tensor_tensor(out_, p_in[:, k, :], -H3[m], q_drive3[:, m, :], ALU.mult, ALU.add)

            def ahead(n, k, step):
                if k == 0:
                    clip_q(n)
                    dve.wait_ge(q_clipped, step + 1)
                    dve.wait_ge(drive_ready, step + 1)
                    q0_3 = q0[:, :].unsqueeze(1).broadcast_to([P, 3, F])
                    dve.tensor_tensor(q_drive3[:, :, :], drive3[:, :, :], q0_3, ALU.add)
                    take_leak(n, 0, q0[:, :])
                    split_tanh(n)
                    less_p(base[:, 0, :], 0, 0)
                    dve.wait_ge(p_off_ready, step + 1)
                    next_p(0)
                    take_cubic(n, q0[:, :])
                    dve.wait_ge(cubic_ready, n + 1)
                    take_pre(0, base[:, 0, :]).then_inc(pre_ready, 1)
                    less_p(base[:, 1, :], 1, 0)
                elif k in (1, 2):
                    dve.wait_ge(q_ready, n + 1)
                    take_leak(n, k, q_in[:, k, :])
                    split_tanh(n)
                    next_p(k)
                    take_cubic(n, q_in[:, k, :])
                    dve.wait_ge(cubic_ready, n + 1)
                    take_pre(k, base[:, k, :]).then_inc(pre_ready, 1)
                    less_p(base[:, k + 1, :], k + 1, SCALE_OF[k + 1])
                else:
                    dve.wait_ge(q_ready, n + 1)
                    take_leak(n, 3, q_in[:, 3, :])
                    dve.tensor_tensor(dq[:, 2, :], q_in[:, 3, :], q0[:, :], ALU.subtract)
                    split_tanh(n)
                    dve.wait_ge(sums_ready, step + 1)
                    dve.tensor_tensor(dq_sum[:, :], dq_sum2[:, :], dq[:, 2, :], ALU.add)
                    dve.tensor_tensor(leak_sum[:, 2, :], leak[:, 3, :], leak_sum[:, 1, :], ALU.add).then_inc(drives_added, 1)
                    take_cubic(n, q_in[:, 3, :])
                    dve.wait_ge(cubic_ready, n + 1)
                    dve.scalar_tensor_tensor(base_last[:, :], dq_sum[:, :], 1.0 / 3.0, base[:, 3, :], ALU.mult,
                                             ALU.add).then_inc(step_sum, 1)
                    dve.scalar_tensor_tensor(p_new[:, :], leak_sum[:, 2, :], DT * EPSILON / 6.0, p_off[:, 1, :],
                                             ALU.mult, ALU.add).then_inc(p_summed, 1)
                    dve.wait_ge(step_sum, step + 1)
                    take_pre(3, base_last[:, :]).then_inc(pre_ready, 1)
                    dve.wait_ge(p_summed, step + 1)
                    dve.tensor_scalar(p_in[:, 0, :], p_new[:, :], CLAMP, -CLAMP, ALU.min, ALU.max).then_inc(p_clipped, 1)

            def close(n, k):
                dve.wait_ge(pre_ready, n + 1)
                dve.wait_ge(coupled, n + 1)
                m = SCALE_OF[k]
                v = lambda t: t.rearrange("p (j b) -> p j b", j=J)
                dve.scalar_tensor_tensor(v(part[:, :]), g_ps[:, :, 1, :], g_lo_scale[:, m:m + 1], v(pre[:, k, :]),
                                         ALU.mult, ALU.add).then_inc(part_ready, 1)
                dve.wait_ge(part_ready, n + 1)
                dve.scalar_tensor_tensor(v(q_in[:, (k + 1) % K, :]), g_ps[:, :, 0, :], g_hi_scale[:, m:m + 1],
                                         v(part[:, :]), ALU.mult, ALU.add).then_inc(q_ready, 1)

            ahead(0, 0, 0)

            def chunk(i, first, last):
                for s in range(CH):
                    for k in range(K):
                        n = SG * i + K * s + k
                        step = CH * i + s
                        close(n, k)
                        if k < K - 1:
                            ahead(n + 1, k + 1, step)
                        elif not (last and s == CH - 1):
                            ahead(n + 1, 0, step + 1)

            over_chunks(dve, chunk)
            clip_q(K * T)


_INS = ["x", "cond_2048", "L0_cond_coupling", "L0_cond_bias"]


def kernel(**inputs):
    import numpy as _np
    import concourse.bacc as _bacc
    from concourse import mybir as _mybir
    from concourse.bass_utils import run_bass_kernel_spmd as _run

    nc = _bacc.Bacc("TRN2", target_bir_lowering=False, num_devices=1)
    arrays, args = {}, []
    for name in _INS:
        a = _np.ascontiguousarray(inputs[name])
        arrays[f"in_{name}"] = a
        args.append(nc.dram_tensor(f"in_{name}", a.shape, _mybir.dt.from_np(a.dtype), kind="ExternalInput").ap())
    shape = tuple(inputs["x"].shape)
    args.append(nc.dram_tensor("out_0", shape, _mybir.dt.float32, kind="ExternalOutput").ap())
    build(nc, *args)
    r = _run(nc, [arrays], core_ids=[0])
    return r.results[0]["out_0"]
```

```python
import concourse.bass as bass
from concourse import mybir
from contextlib import ExitStack


fp32 = mybir.dt.float32
fp16 = mybir.dt.float16
u32 = mybir.dt.uint32
ALU = mybir.AluOpType
ACT = mybir.ActivationFunctionType
AX = mybir.AxisListType

DT, EPSILON, ALPHA, BETA, CLAMP = 0.01, 0.08, 0.7, 0.8, 20.0
LO = 2048.0
H3 = [0.5 * DT, DT, DT / 6]
H_OF = [0, 0, 1, 2]
G_TIMES = [H3[m] / H3[0] for m in H_OF]


def build(nc, x, cond, coupling, bias, out):
    B, T, N = x.shape
    P = 128
    J = N // P
    F = J * B
    K = 4
    CH = 4
    NCH = T // CH
    ROWS = B * CH
    SG = K * CH

    x_chunks = x.rearrange("b (c t) n -> c b t n", t=CH)
    out_chunks = out.rearrange("b (c t) (h jj n) -> c jj b t h n", t=CH, jj=2, n=P)

    ctx = ExitStack()
    with ctx:
        def sb(name, shape, dt=fp32):
            return ctx.enter_context(nc.sbuf_tensor(name, shape, dt))

        def bank(name):
            return ctx.enter_context(nc.psum_tensor(name, [P, 512], fp32))

        def sem(name):
            return ctx.enter_context(nc.semaphore(name))

        ident = sb("ident", [P, P])
        c_nat = sb("c_nat", [P, J, N])
        w_scaled = sb("w_scaled", [P, N])
        w_rest = sb("w_rest", [P, N])
        w_hi = sb("w_hi", [P, J, N], fp16)
        w_lo = sb("w_lo", [P, J, N], fp16)
        c_top = sb("c_top", [P, 4])
        inv_s = sb("inv_s", [P, 1])
        s_up = sb("s_up", [P, 1])
        scales = sb("scales", [P, 4])
        bounds = sb("bounds", [P, 2])
        cond_nat = sb("cond_nat", [B, N])
        bias_nat = sb("bias_nat", [J, P])
        bias3 = sb("bias3", [P, 3, F])

        x_nat = sb("x_nat", [ROWS, N])
        x_t = sb("x_t", [P, CH, F])
        x3 = sb("x3", [P, 3, F])
        drive3 = sb("drive3", [P, 3, F])
        y_t = sb("y_t", [P, F * CH])
        y_nat = sb("y_nat", [P, J // 2, P])

        q_in = sb("q_in", [P, K, F])
        q0 = sb("q0", [P, F])
        p_in = sb("p_in", [P, K, F])
        p_new = sb("p_new", [P, F])
        t_hilo = sb("t_hilo", [P, J, 2, B], fp16)
        t_full = sb("t_full", [P, F])
        spare = sb("spare", [P, 2])
        t_lo_top = sb("t_lo_top", [P, 2])
        q_sq = sb("q_sq", [P, F])
        cubic = sb("cubic", [P, F])
        q_drive3 = sb("q_drive3", [P, 3, F])
        base = sb("base", [P, K, F])
        pre = sb("pre", [P, K, F])
        part = sb("part", [P, F])
        leak = sb("leak", [P, K, F])
        alpha3 = sb("alpha3", [P, 3, F])
        p_off = sb("p_off", [P, 2, F])
        base_last = sb("base_last", [P, F])
        slope0 = sb("slope0", [P, F])
        dq = sb("dq", [P, 2, F])
        dq_less = sb("dq_less", [P, F])
        dq_part = sb("dq_part", [P, 2, F])
        q_middle = sb("q_middle", [P, F])
        q_last = sb("q_last", [P, F])
        thirds = sb("thirds", [P, 2, F])
        leak_twice = sb("leak_twice", [P, 2, F])
        leak_sum = sb("leak_sum", [P, 4, F])
        q_true = sb("q_true", [P, F])

        g_banks = [bank(f"g_ps{i}") for i in range(4)]
        g_ps = [[g_banks[2 * odd + h][:, 0:F].rearrange("p (j part b) -> p j part b", j=J // 2, part=2)
                 for h in range(2)] for odd in range(2)]
        wt_ps = g_banks[0:2]
        x_ps = bank("x_ps")[:, 0:F * CH]
        y_ps = bank("y_ps")[:, 0:J // 2 * P].rearrange("p (h n) -> p h n", n=P)
        setup_ps = bank("setup_ps")[:, 0:F + J]

        ident_zeroed, ident_ready = sem("ident_zeroed"), sem("ident_ready")
        coupling_in, cond_in, bias_in = sem("coupling_in"), sem("cond_in"), sem("bias_in")
        top_of_rows, top_of_all, setup_chain = sem("top_of_rows"), sem("top_of_all"), sem("setup_chain")
        weights_turned, weights_taken = sem("weights_turned"), sem("weights_taken")
        setup_turned, bias_ready, scales_ready = sem("setup_turned"), sem("bias_ready"), sem("scales_ready")
        x_in, x_turned = sem("x_in"), sem("x_turned")
        y_turned, y_out_ready, y_stored = sem("y_turned"), sem("y_out_ready"), sem("y_stored")
        x_next, drive_ready, q_clipped, p_clipped = sem("x_next"), sem("drive_ready"), sem("q_clipped"), sem("p_clipped")
        p_off_ready, q_drive_ready, q_unscaled = sem("p_off_ready"), sem("q_drive_ready"), sem("q_unscaled")
        y_done, sum_chain, q_last_ready, leaks_summed = (sem("y_done"), sem("sum_chain"), sem("q_last_ready"),
                                                         sem("leaks_summed"))
        base_ready, slope_ready, p_summed = sem("base_ready"), sem("slope_ready"), sem("p_summed")
        leak_ready, sq_ready, cubic_ready, pre_ready = (sem("leak_ready"), sem("sq_ready"), sem("cubic_ready"),
                                                        sem("pre_ready"))
        q_ready, th_hi, th_full, th_lo = ([sem(f"{name}{h}") for h in range(2)]
                                          for name in ("q_ready", "th_hi", "th_full", "th_lo"))
        coupled, part_ready = ([sem(f"{name}{h}") for h in range(2)] for name in ("coupled", "part_ready"))

        HJ, HF = J // 2, F // 2

        def half(t, h):
            return t[:, h * HF:(h + 1) * HF].rearrange("p (j b) -> p j b", j=HJ)

        def over_chunks(eng, body):
            body(0, True, False)
            with eng.Fori(1, NCH - 1) as i:
                body(i, False, False)
            body(NCH - 1, False, True)

        block = ctx.enter_context(nc.Block())

        @block.sync
        def _(sp):
            sp.dma_start(c_nat[:, :, :], coupling.rearrange("(j p) m -> p j m", p=P)).then_inc(coupling_in, 16)
            sp.dma_start(cond_nat[:, :], cond).then_inc(cond_in, 16)
            sp.dma_start(bias_nat[:, :], bias.rearrange("(j p) -> j p", p=P)).then_inc(bias_in, 16)
            sp.dma_start(x_nat[:, :], x_chunks[0]).then_inc(x_in, 16)

            def chunk(i, first, last):
                if not last:
                    sp.wait_ge(x_turned, i + 1)
                if not first:
                    store(i - 1)
                    sp.wait_ge(y_stored, 32 * i)
                if not last:
                    sp.dma_start(x_nat[:, :], x_chunks[i + 1]).then_inc(x_in, 16)

            def store(c):
                sp.wait_ge(y_out_ready, c + 1)
                for jj in range(2):
                    sp.dma_start(out_chunks[c, jj], y_nat[jj * ROWS:(jj + 1) * ROWS, :, :]).then_inc(y_stored, 16)

            over_chunks(sp, chunk)
            store(NCH - 1)
            sp.wait_ge(y_stored, 32 * NCH)

        @block.tensor
        def _(pe):
            pe.wait_ge(ident_ready, 1)
            pe.wait_ge(cond_in, 16)
            for j in range(J):
                pe.transpose(setup_ps[:, j * B:(j + 1) * B], cond_nat[:, j * P:(j + 1) * P], ident[0:B, 0:B])
            pe.wait_ge(bias_in, 16)
            pe.transpose(setup_ps[:, F:F + J], bias_nat[:, :], ident[0:J, 0:J]).then_inc(setup_turned, 1)
            pe.wait_ge(coupling_in, 16)
            for k in range(J):
                if k >= 2:
                    pe.wait_ge(weights_taken, k - 1)
                for j in range(J):
                    last = pe.transpose(wt_ps[k % 2][:, j * P:(j + 1) * P], c_nat[:, j, k * P:(k + 1) * P], ident[:, :])
                last.then_inc(weights_turned, 1)

            def turn_x(c):
                for j in range(J):
                    last = pe.transpose(x_ps[:, j * ROWS:(j + 1) * ROWS], x_nat[:, j * P:(j + 1) * P],
                                        ident[0:ROWS, 0:ROWS])
                last.then_inc(x_turned, 1)

            def turn_y(c):
                pe.wait_ge(y_done, CH * (c + 1))
                for h in range(J // 2):
                    last = pe.transpose(y_ps[:, h, :], y_t[:, h * P:(h + 1) * P], ident[:, :])
                last.then_inc(y_turned, 1)

            pe.wait_ge(x_in, 16)
            turn_x(0)
            pe.wait_ge(weights_taken, J)

            def block_products(odd, j, k, w, out_cols, t_cols, start=False, stop=False):
                return pe.matmul(g_ps[odd][j // HJ][:, j % HJ, out_cols, :], w[:, k, j * P:(j + 1) * P], t_hilo[:, k, t_cols, :],
                                 start=start, stop=stop, skip_group_check=True)

            def couple(n, odd):
                for h in range(2):
                    pe.wait_ge(th_hi[h], n + 1)
                    for j in range(J):
                        for k in range(h * HJ, (h + 1) * HJ):
                            block_products(odd, j, k, w_lo, 1, 0, start=(j % HJ == 0 and k == 0))
                for jh in range(2):
                    for h in range(2):
                        if jh == 0:
                            pe.wait_ge(th_lo[h], n + 1)
                        for j in range(jh * HJ, (jh + 1) * HJ):
                            for k in range(h * HJ, (h + 1) * HJ):
                                last = block_products(odd, j, k, w_hi, slice(0, 2), slice(0, 2), stop=(k == J - 1))
                    last.then_inc(coupled[jh], 1)

            def chunk(i, first, last):
                for s in range(CH):
                    for k in range(K):
                        if s == CH - 1 and k == 1 and not last:
                            pe.wait_ge(th_hi[0], SG * i + K * s + k + 1)
                            pe.wait_ge(x_in, 16 * (i + 2))
                        couple(SG * i + K * s + k, k % 2)
                        if s == 0 and k == 2 and not first:
                            turn_y(i - 1)
                        if s == CH - 1 and k == 1 and not last:
                            turn_x(i + 1)

            over_chunks(pe, chunk)
            turn_y(NCH - 1)

        @block.scalar
        def _(act):
            act.preload_act_table(ACT.Tanh)
            act.wait_ge(scales_ready, 1)
            scale_regs = []
            for m in range(4):
                reg = act.alloc_register(f"scale{m}")
                act.reg_load(reg, scales[0:1, m:m + 1].bitcast(u32))
                scale_regs.append(reg)
            one_over_s, s_h = scale_regs[0], scale_regs[1:]

            def take_x(step, s):
                src = x_ps[:, s:F * CH:CH]
                act.copy(x_t[:, s, :], src)
                for m in range(3):
                    last = act.activation(x3[:, m, :], src, ACT.Copy, scale=s_h[m])
                last.then_inc(x_next, 1)

            act.wait_ge(x_turned, 1)
            take_x(0, 0)

            def tanh_parts(n, k, step):
                for h in range(2):
                    act.wait_ge(q_ready[h], n + 1)
                    act.activation(t_hilo[:, h * HJ:(h + 1) * HJ, 0, :], half(q_in[:, k, :], h), ACT.Tanh,
                                   scale=one_over_s).then_inc(th_hi[h], 1)
                    act.activation(t_full[:, h * HF:(h + 1) * HF], q_in[:, k, h * HF:(h + 1) * HF], ACT.Tanh,
                                   scale=one_over_s).then_inc(th_full[h], 1)
                if k == 0:
                    act.wait_ge(q_clipped, step + 1)
                act.activation(q_sq[:, :], q0[:, :] if k == 0 else q_in[:, k, :], ACT.Square,
                               scale=one_over_s).then_inc(sq_ready, 1)
                if k == 0:
                    act.activation(q_true[:, :], q0[:, :], ACT.Copy, scale=one_over_s).then_inc(q_unscaled, 1)

            def chunk(i, first, last):
                for s in range(CH):
                    for k in range(K):
                        step = CH * i + s
                        tanh_parts(SG * i + K * s + k, k, step)
                        if k == 2 and not (last and s == CH - 1):
                            act.wait_ge(drive_ready, step + 1)
                            if s == CH - 1:
                                act.wait_ge(x_turned, i + 2)
                            take_x(step + 1, (s + 1) % CH)
                        if s == 0 and k == 3 and not first:
                            take_y(i - 1)

            def take_y(c):
                act.wait_ge(y_turned, c + 1)
                act.copy(y_nat[:, :, :], y_ps[:, :, :]).then_inc(y_out_ready, 1)

            over_chunks(act, chunk)
            act.wait_ge(y_stored, 32 * (NCH - 1))
            act.wait_ge(q_clipped, T + 1)
            act.activation(q_true[:, :], q0[:, :], ACT.Copy, scale=one_over_s).then_inc(q_unscaled, 1)
            take_y(NCH - 1)

        LINKS = 11

        @block.gpsimd
        def _(pool):
            nc.gpsimd.memset(ident[:, :], 0.0).then_inc(ident_zeroed, 1)
            pool.wait_ge(ident_zeroed, 1)
            nc.gpsimd.affine_select(out=ident[:, :], in_=ident[:, :], compare_op=ALU.not_equal, fill=1.0, base=0,
                                    pattern=[[-1, P]], channel_multiplier=1).then_inc(ident_ready, 1)
            pool.wait_ge(top_of_rows, 1)
            nc.gpsimd.partition_all_reduce(c_top[:, 3:4], c_top[:, 2:3], P, bass.bass_isa.ReduceOp.max).then_inc(top_of_all, 1)
            pool.wait_ge(bias_ready, 1)

            def add_bias(step):
                pool.wait_ge(x_next, step + 1)
                pool.tensor_tensor(drive3[:, :, :], x3[:, :, :], bias3[:, :, :], ALU.add).then_inc(drive_ready, 1)

            add_bias(0)

            def finish_step(step, s):
                pool.wait_ge(q_unscaled, step + 2)
                pool.tensor_tensor(y_t[:, s:F * CH:CH], q_true[:, :], x_t[:, s, :], ALU.add).then_inc(y_done, 1)

            def chunk(i, first, last):
                for s in range(CH):
                    step = CH * i + s
                    n = SG * i + K * s
                    links = [0]

                    def link(ins):
                        links[0] += 1
                        ins.then_inc(sum_chain, 1)
                        return LINKS * step + links[0]

                    def add(dst, a, b):
                        return pool.tensor_tensor(dst, a, b, ALU.add)

                    def less(dst, a, b):
                        return pool.tensor_tensor(dst, a, b, ALU.subtract)

                    def times(dst, a, b):
                        return pool.tensor_tensor(dst, a, b, ALU.mult)

                    pool.wait_ge(p_clipped, step + 1)
                    add(p_off[:, :, :], p_in[:, 0, :].unsqueeze(1).broadcast_to([P, 2, F]),
                        alpha3[:, 0:2, :]).then_inc(p_off_ready, 1)
                    pool.wait_ge(q_clipped, step + 1)
                    pool.wait_ge(drive_ready, step + 1)
                    add(q_drive3[:, :, :], drive3[:, :, :],
                        q0[:, :].unsqueeze(1).broadcast_to([P, 3, F])).then_inc(q_drive_ready, 1)
                    pool.wait_ge(leak_ready, n + 1)
                    link(add(leak_sum[:, 0, :], leak[:, 0, :], alpha3[:, 2, :]))
                    if not (first and s == 0):
                        finish_step(step - 1, (s - 1) % CH)
                    pool.wait_ge(leak_ready, n + 2)
                    step_1 = link(less(dq[:, 0, :], q_in[:, 1, :], q0[:, :]))
                    twice = link(add(leak_twice[:, 0, :], leak[:, 1, :], leak[:, 1, :]))
                    pool.wait_ge(sum_chain, step_1)
                    step_1 = link(less(dq_less[:, :], dq[:, 0, :], q0[:, :]))
                    pool.wait_ge(sum_chain, twice)
                    link(add(leak_sum[:, 1, :], leak_twice[:, 0, :], leak_sum[:, 0, :]))
                    pool.wait_ge(sum_chain, step_1)
                    step_1 = link(times(dq_part[:, 0, :], dq_less[:, :], thirds[:, 0, :]))
                    pool.wait_ge(sum_chain, step_1)
                    link(add(q_middle[:, :], dq_part[:, 0, :], q_drive3[:, 2, :]))
                    pool.wait_ge(leak_ready, n + 3)
                    step_2 = link(less(dq[:, 1, :], q_in[:, 2, :], q0[:, :]))
                    pool.wait_ge(sum_chain, step_2)
                    step_2 = link(times(dq_part[:, 1, :], dq[:, 1, :], thirds[:, 1, :]))
                    pool.wait_ge(sum_chain, step_2)
                    add(q_last[:, :], dq_part[:, 1, :], q_middle[:, :]).then_inc(q_last_ready, 1)
                    twice = link(add(leak_twice[:, 1, :], leak[:, 2, :], leak[:, 2, :]))
                    pool.wait_ge(sum_chain, twice)
                    twice = link(add(leak_sum[:, 2, :], leak_twice[:, 1, :], leak_sum[:, 1, :]))
                    pool.wait_ge(leak_ready, n + 4)
                    pool.wait_ge(sum_chain, twice)
                    add(leak_sum[:, 3, :], leak[:, 3, :], leak_sum[:, 2, :]).then_inc(leaks_summed, 1)
                    if not (last and s == CH - 1):
                        add_bias(step + 1)
                    assert links[0] == LINKS

            over_chunks(pool, chunk)
            finish_step(T - 1, CH - 1)

        @block.vector
        def _(dve):
            links = [0]

            def link(ins):
                links[0] += 1
                ins.then_inc(setup_chain, 1)
                dve.wait_ge(setup_chain, links[0])

            dve.wait_ge(coupling_in, 16)
            link(dve.tensor_reduce(c_top[:, 0:1], c_nat[:, :, :], AX.XY, ALU.max))
            link(dve.tensor_reduce(c_top[:, 1:2], c_nat[:, :, :], AX.XY, ALU.min))
            dve.scalar_tensor_tensor(c_top[:, 2:3], c_top[:, 1:2], -1.0, c_top[:, 0:1], ALU.mult,
                                     ALU.max).then_inc(top_of_rows, 1)
            dve.wait_ge(top_of_all, 1)
            link(dve.tensor_scalar(inv_s[:, :], c_top[:, 3:4], H3[0], 2.0 ** -60, ALU.mult, ALU.max))
            link(dve.tensor_scalar(s_up[:, :].bitcast(u32), inv_s[:, :].bitcast(u32), 0x7F800000, None, ALU.bitwise_and))
            link(dve.tensor_scalar(inv_s[:, :], s_up[:, :], 2.0 ** -14, None, ALU.mult))
            link(dve.reciprocal(s_up[:, :], inv_s[:, :]))
            for m in range(3):
                link(dve.tensor_scalar(scales[:, 1 + m:2 + m], s_up[:, :], H3[m], None, ALU.mult))
            link(dve.tensor_scalar(bounds[:, 0:1], s_up[:, :], CLAMP, None, ALU.mult))
            link(dve.tensor_scalar(bounds[:, 1:2], s_up[:, :], -CLAMP, None, ALU.mult))
            dve.tensor_copy(scales[:, 0:1], inv_s[:, :]).then_inc(scales_ready, 1)
            dve.wait_ge(setup_turned, 1)
            for m in range(3):
                bias_cols = setup_ps[:, F:F + J].unsqueeze(2).broadcast_to([P, J, B])
                link(dve.tensor_scalar(bias3[:, m, :].rearrange("p (j b) -> p j b", j=J), bias_cols, scales[:, 1 + m:2 + m], None,
                                       ALU.mult))
            for m, a in enumerate((H3[0] * EPSILON * ALPHA, H3[1] * EPSILON * ALPHA, 6 * ALPHA)):
                link(dve.memset(part[:, :], a))
                link(dve.tensor_scalar(alpha3[:, m, :], part[:, :], s_up[:, 0:1], None, ALU.mult))
            for m in range(2):
                link(dve.memset(thirds[:, m, :], (m + 1) / 3.0))
            dve.tensor_scalar(p_in[:, 0, :], setup_ps[:, 0:F], s_up[:, 0:1], None, ALU.mult).then_inc(p_clipped, 1)
            dve.tensor_scalar(q_in[:, 0, :], setup_ps[:, 0:F], s_up[:, 0:1], None, ALU.mult).then_inc(bias_ready, 1)
            for k in range(J):
                dve.wait_ge(weights_turned, k + 1)
                link(dve.tensor_scalar(w_scaled[:, :], wt_ps[k % 2][:, :], H3[0], s_up[:, 0:1], ALU.mult, ALU.mult))
                link(dve.tensor_copy(w_hi[:, k, :], w_scaled[:, :]))
                link(dve.scalar_tensor_tensor(w_rest[:, :], w_hi[:, k, :], -1.0, w_scaled[:, :], ALU.mult, ALU.add))
                dve.tensor_scalar(w_lo[:, k, :], w_rest[:, :], LO, None, ALU.mult).then_inc(weights_taken, 1)
                dve.wait_ge(weights_taken, k + 1)
            for h in range(2):
                dve.sem_inc(q_ready[h], 1)

            def clip_q(n):
                dve.wait_ge(q_ready[1], n + 1)
                dve.tensor_scalar(q0[:, :], q_in[:, 0, :], bounds[:, 0:1], bounds[:, 1:2], ALU.min,
                                  ALU.max).then_inc(q_clipped, 1)

            def clip_p():
                dve.tensor_scalar(p_in[:, 0, :], p_new[:, :], bounds[:, 0:1], bounds[:, 1:2], ALU.min,
                                  ALU.max).then_inc(p_clipped, 1)

            def split_tanh(n, h):
                carry(th_full[h], n, h)
                dve.tensor_tensor_reduce(t_hilo[:, h * HJ:(h + 1) * HJ, 1, :], half(t_full, h),
                                         t_hilo[:, h * HJ:(h + 1) * HJ, 0, :], LO, 0.0, ALU.subtract, ALU.max,
                                         t_lo_top[:, h:h + 1]).then_inc(th_lo[h], 1)

            def take_leak(k, q):
                dve.scalar_tensor_tensor(leak[:, k, :], p_in[:, k, :], -BETA, q, ALU.mult,
                                         ALU.add).then_inc(leak_ready, 1)

            def next_p(k):
                return dve.scalar_tensor_tensor(p_in[:, k + 1, :], leak[:, k, :], H3[H_OF[k]] * EPSILON,
                                                p_off[:, H_OF[k], :], ALU.mult, ALU.add)

            def less_p(k):
                on = q_last[:, :] if k == 3 else q_drive3[:, H_OF[k], :]
                ins = dve.scalar_tensor_tensor(base[:, k, :], p_in[:, k, :], -H3[H_OF[k]], on, ALU.mult, ALU.add)
                if k == K - 1:
                    ins.then_inc(base_ready, 1)

            def carry(semaphore, n, h):
                dve.wait_ge(semaphore, n + 1)
                dve.memset(spare[:, h:h + 1], 0.0)

            def take_cubic(n, q):
                dve.wait_ge(sq_ready, n + 1)
                dve.scalar_tensor_tensor(cubic[:, :], q_sq[:, :], -3.0, q, ALU.add, ALU.mult).then_inc(cubic_ready, 1)

            def take_pre(k, base_k):
                dve.scalar_tensor_tensor(pre[:, k, :], cubic[:, :], -H3[H_OF[k]] / 3.0, base_k, ALU.mult,
                                         ALU.add).then_inc(pre_ready, 1)

            def ahead(n, k, step, started=True):
                if k == 0:
                    if started:
                        dve.wait_ge(p_summed, step)
                        clip_p()
                    clip_q(n)
                    split_tanh(n, 0)
                    dve.wait_ge(q_clipped, step + 1)
                    take_leak(k, q0[:, :])
                    dve.wait_ge(drive_ready, step + 1)
                    dve.scalar_tensor_tensor(slope0[:, :], p_in[:, 0, :], -H3[0], drive3[:, 0, :], ALU.mult,
                                             ALU.add).then_inc(slope_ready, 1)
                    split_tanh(n, 1)
                    take_cubic(n, q0[:, :])
                    dve.wait_ge(slope_ready, step + 1)
                    dve.tensor_tensor(base[:, 0, :], slope0[:, :], q0[:, :], ALU.add).then_inc(base_ready, 1)
                    dve.wait_ge(base_ready, 2 * step + 1)
                    take_pre(k, base[:, k, :])
                    dve.wait_ge(p_off_ready, step + 1)
                    next_p(k)
                elif k < K - 1:
                    if k == 1:
                        dve.wait_ge(q_drive_ready, step + 1)
                    less_p(k)
                    dve.wait_ge(q_ready[1], n + 1)
                    take_leak(k, q_in[:, k, :])
                    split_tanh(n, 0)
                    split_tanh(n, 1)
                    take_cubic(n, q_in[:, k, :])
                    dve.wait_ge(leak_ready, n + 1)
                    next_p(k)
                    dve.wait_ge(cubic_ready, n + 1)
                    take_pre(k, base[:, k, :])
                else:
                    dve.wait_ge(q_last_ready, step + 1)
                    less_p(k)
                    dve.wait_ge(q_ready[1], n + 1)
                    take_leak(k, q_in[:, k, :])
                    dve.wait_ge(base_ready, 2 * step + 2)
                    dve.scalar_tensor_tensor(base_last[:, :], q_in[:, 3, :], 1.0 / 3.0, base[:, 3, :], ALU.mult,
                                             ALU.add)
                    split_tanh(n, 0)
                    split_tanh(n, 1)
                    take_cubic(n, q_in[:, k, :])
                    dve.wait_ge(cubic_ready, n + 1)
                    take_pre(k, base_last[:, :])
                    dve.wait_ge(leaks_summed, step + 1)
                    dve.scalar_tensor_tensor(p_new[:, :], leak_sum[:, 3, :], DT * EPSILON / 6.0, p_in[:, 0, :],
                                             ALU.mult, ALU.add).then_inc(p_summed, 1)

            def close(n, k):
                for h in range(2):
                    if h == 0:
                        dve.wait_ge(pre_ready, n + 1)
                    dve.wait_ge(coupled[h], n + 1)
                    dve.scalar_tensor_tensor(half(part, h), g_ps[k % 2][h][:, :, 1, :], G_TIMES[k] / LO,
                                             half(pre[:, k, :], h), ALU.mult, ALU.add).then_inc(part_ready[h], 1)
                for h in range(2):
                    dve.wait_ge(part_ready[h], n + 1)
                    dve.scalar_tensor_tensor(half(q_in[:, (k + 1) % K, :], h), g_ps[k % 2][h][:, :, 0, :], G_TIMES[k],
                                             half(part, h), ALU.mult, ALU.add).then_inc(q_ready[h], 1)

            ahead(0, 0, 0, started=False)

            def chunk(i, first, last):
                for s in range(CH):
                    for k in range(K):
                        n = SG * i + K * s + k
                        step = CH * i + s
                        close(n, k)
                        if k < K - 1:
                            ahead(n + 1, k + 1, step)
                        elif not (last and s == CH - 1):
                            ahead(n + 1, 0, step + 1)

            over_chunks(dve, chunk)
            clip_q(K * T)


_INS = ["x", "cond_2048", "L0_cond_coupling", "L0_cond_bias"]


def kernel(**inputs):
    import numpy as _np
    import concourse.bacc as _bacc
    from concourse import mybir as _mybir
    from concourse.bass_utils import run_bass_kernel_spmd as _run

    nc = _bacc.Bacc("TRN2", target_bir_lowering=False, num_devices=1)
    arrays, args = {}, []
    for name in _INS:
        a = _np.ascontiguousarray(inputs[name])
        arrays[f"in_{name}"] = a
        args.append(nc.dram_tensor(f"in_{name}", a.shape, _mybir.dt.from_np(a.dtype), kind="ExternalInput").ap())
    shape = tuple(inputs["x"].shape)
    args.append(nc.dram_tensor("out_0", shape, _mybir.dt.float32, kind="ExternalOutput").ap())
    build(nc, *args)
    r = _run(nc, [arrays], core_ids=[0])
    return r.results[0]["out_0"]
```

```python
import concourse.bass as bass
from concourse import mybir
from contextlib import ExitStack


fp32 = mybir.dt.float32
fp16 = mybir.dt.float16
u32 = mybir.dt.uint32
ALU = mybir.AluOpType
ACT = mybir.ActivationFunctionType
AX = mybir.AxisListType

DT, EPSILON, ALPHA, BETA, CLAMP = 0.01, 0.08, 0.7, 0.8, 20.0
LO = 2048.0
H3 = [0.5 * DT, DT, DT / 6]
H_OF = [0, 0, 1, 2]
G_TIMES = [H3[m] / H3[0] for m in H_OF]

ONE_THIRD, TWO_THIRDS = 11184810 / 2.0 ** 25, 11184811 / 2.0 ** 24


def build(nc, x, cond, coupling, bias, out):
    B, T, N = x.shape
    P = 128
    J = N // P
    F = J * B
    K = 4
    CH = 8
    NCH = T // CH
    AT_ONCE = 3
    assert (NCH - 2) % AT_ONCE == 0
    ROWS = B * CH
    SG = K * CH
    JJ = P // ROWS
    YJ = J // JJ

    x_chunks = x.rearrange("b (c t) n -> c b t n", t=CH)
    out_chunks = out.rearrange("b (c t) (h jj n) -> c jj b t h n", t=CH, jj=JJ, n=P)

    ctx = ExitStack()
    with ctx:
        def sb(name, shape, dt=fp32):
            return ctx.enter_context(nc.sbuf_tensor(name, shape, dt))

        def bank(name):
            return ctx.enter_context(nc.psum_tensor(name, [P, 512], fp32))

        def sem(name):
            return ctx.enter_context(nc.semaphore(name))

        SPARES = 24
        ident = sb("ident", [P, P])
        c_nat = sb("c_nat", [P, J, N])
        w_scaled = sb("w_scaled", [P, N])
        w_rest = sb("w_rest", [P, N])
        w_hi = sb("w_hi", [P, J, N], fp16)
        w_lo = sb("w_lo", [P, J, N], fp16)
        c_top = sb("c_top", [P, 4])
        inv_s = sb("inv_s", [P, 1])
        s_up = sb("s_up", [P, 1])
        scales = sb("scales", [P, 4])
        bounds = sb("bounds", [P, 2])
        cond_nat = sb("cond_nat", [B, N])
        bias_nat = sb("bias_nat", [J, P])
        bias3 = sb("bias3", [P, 3, F])

        x_nat = sb("x_nat", [ROWS, N])
        x_t = sb("x_t", [P, CH, F])
        x3 = sb("x3", [P, 3, F])
        drive3 = sb("drive3", [P, 3, F])
        y_t = sb("y_t", [P, F * CH])
        y_nat = sb("y_nat", [P, YJ, P])

        q_in = sb("q_in", [P, K, F])
        q0 = sb("q0", [P, F])
        p_in = sb("p_in", [P, K, F])
        p_new = sb("p_new", [P, F])
        t_hilo = sb("t_hilo", [P, J, 2, B], fp16)
        t_full = sb("t_full", [P, F])
        spare = sb("spare", [P, SPARES])
        t_lo_top = sb("t_lo_top", [P, 2])
        q_sq = sb("q_sq", [P, F])
        cubic = sb("cubic", [P, F])
        q_drive = sb("q_drive", [P, 2, F])
        slope0 = sb("slope0", [P, F])
        base = sb("base", [P, K, F])
        pre = sb("pre", [P, K, F])
        part = sb("part", [P, F])
        leak = sb("leak", [P, K, F])
        alpha3 = sb("alpha3", [P, 3, F])
        p_off = sb("p_off", [P, 2, F])
        base_last = sb("base_last", [P, F])
        dq = sb("dq", [P, F])
        dq_third = sb("dq_third", [P, F])
        q_middle = sb("q_middle", [P, F])
        q_last = sb("q_last", [P, F])
        thirds = sb("thirds", [P, F])
        leak_twice = sb("leak_twice", [P, 2, F])
        leak_sum = sb("leak_sum", [P, 3, F])
        p_gain = sb("p_gain", [P, F])
        p_moved = sb("p_moved", [P, F])
        p_most = sb("p_most", [P, F])
        pool_spare = sb("pool_spare", [P, CH])
        q_true = sb("q_true", [P, F])

        g_banks = [bank(f"g_ps{i}") for i in range(4)]
        g_ps = [[g_banks[2 * odd + h][:, 0:F].rearrange("p (j part b) -> p j part b", j=J // 2, part=2)
                 for h in range(2)] for odd in range(2)]
        wt_ps = g_banks[0:2]
        x_ps = bank("x_ps")[:, 0:F * CH]
        y_ps = bank("y_ps")[:, 0:YJ * P].rearrange("p (h n) -> p h n", n=P)
        setup_ps = bank("setup_ps")[:, 0:F + J]

        ident_zeroed, ident_ready = sem("ident_zeroed"), sem("ident_ready")
        coupling_in, cond_in, bias_in = sem("coupling_in"), sem("cond_in"), sem("bias_in")
        top_of_rows, top_of_all, setup_chain = sem("top_of_rows"), sem("top_of_all"), sem("setup_chain")
        weights_turned, weights_taken = sem("weights_turned"), sem("weights_taken")
        setup_turned, bias_ready, scales_ready = sem("setup_turned"), sem("bias_ready"), sem("scales_ready")
        x_in, x_turned = sem("x_in"), sem("x_turned")
        y_turned, y_out_ready, y_stored = sem("y_turned"), sem("y_out_ready"), sem("y_stored")
        x_next, drive_ready = sem("x_next"), sem("drive_ready")
        q_clipped, p_clipped = sem("q_clipped"), sem("p_clipped")
        p_off_ready, q_drive_ready, q_unscaled = sem("p_off_ready"), sem("q_drive_ready"), sem("q_unscaled")
        y_done, sum_chain = sem("y_done"), sem("sum_chain")
        q_middle_ready, q_last_ready, p_most_ready = sem("q_middle_ready"), sem("q_last_ready"), sem("p_most_ready")
        base_ready, p1_ready, p_summed = sem("base_ready"), sem("p1_ready"), sem("p_summed")
        leak_ready, sq_ready, cubic_ready = sem("leak_ready"), sem("sq_ready"), sem("cubic_ready")
        q_ready, th_hi, th_full, th_lo = ([sem(f"{name}{h}") for h in range(2)]
                                          for name in ("q_ready", "th_hi", "th_full", "th_lo"))
        pre_ready, coupled, part_ready = ([sem(f"{name}{h}") for h in range(2)]
                                          for name in ("pre_ready", "coupled", "part_ready"))

        HJ, HF = J // 2, F // 2

        def half(t, h):
            return t[:, h * HF:(h + 1) * HF].rearrange("p (j b) -> p j b", j=HJ)

        def over_chunks(eng, body, at_once=AT_ONCE):
            body(0, True, False)
            with eng.Fori(1, NCH - 1, at_once) as i:
                for u in range(at_once):
                    body(i + u if u else i, False, False)
            body(NCH - 1, False, True)

        block = ctx.enter_context(nc.Block())

        @block.sync
        def _(sp):
            sp.dma_start(c_nat[:, :, :], coupling.rearrange("(j p) m -> p j m", p=P)).then_inc(coupling_in, 16)
            sp.dma_start(cond_nat[:, :], cond).then_inc(cond_in, 16)
            sp.dma_start(bias_nat[:, :], bias.rearrange("(j p) -> j p", p=P)).then_inc(bias_in, 16)
            sp.dma_start(x_nat[:, :], x_chunks[0]).then_inc(x_in, 16)

            def chunk(i, first, last):
                if not last:
                    sp.wait_ge(x_turned, i + 1)
                if not first:
                    store(i - 1)
                    sp.wait_ge(y_stored, 16 * JJ * i)
                if not last:
                    sp.dma_start(x_nat[:, :], x_chunks[i + 1]).then_inc(x_in, 16)

            def store(c):
                sp.wait_ge(y_out_ready, c + 1)
                for jj in range(JJ):
                    sp.dma_start(out_chunks[c, jj], y_nat[jj * ROWS:(jj + 1) * ROWS, :, :]).then_inc(y_stored, 16)

            over_chunks(sp, chunk, at_once=1)
            store(NCH - 1)
            sp.wait_ge(y_stored, 16 * JJ * NCH)

        @block.tensor
        def _(pe):
            pe.wait_ge(ident_ready, 1)
            pe.wait_ge(cond_in, 16)
            for j in range(J):
                pe.transpose(setup_ps[:, j * B:(j + 1) * B], cond_nat[:, j * P:(j + 1) * P], ident[0:B, 0:B])
            pe.wait_ge(bias_in, 16)
            pe.transpose(setup_ps[:, F:F + J], bias_nat[:, :], ident[0:J, 0:J]).then_inc(setup_turned, 1)
            pe.wait_ge(coupling_in, 16)
            for k in range(J):
                if k >= 2:
                    pe.wait_ge(weights_taken, k - 1)
                for j in range(J):
                    last = pe.transpose(wt_ps[k % 2][:, j * P:(j + 1) * P], c_nat[:, j, k * P:(k + 1) * P], ident[:, :])
                last.then_inc(weights_turned, 1)

            def turn_x(c):
                for j in range(J):
                    last = pe.transpose(x_ps[:, j * ROWS:(j + 1) * ROWS], x_nat[:, j * P:(j + 1) * P],
                                        ident[0:ROWS, 0:ROWS])
                last.then_inc(x_turned, 1)

            def turn_y(c):
                pe.wait_ge(y_done, CH * (c + 1))
                for h in range(YJ):
                    last = pe.transpose(y_ps[:, h, :], y_t[:, h * P:(h + 1) * P], ident[:, :])
                last.then_inc(y_turned, 1)

            pe.wait_ge(x_in, 16)
            turn_x(0)
            pe.wait_ge(weights_taken, J)

            def block_products(odd, j, k, w, out_cols, t_cols, start=False, stop=False):
                return pe.matmul(g_ps[odd][j // HJ][:, j % HJ, out_cols, :], w[:, k, j * P:(j + 1) * P],
                                 t_hilo[:, k, t_cols, :], start=start, stop=stop, skip_group_check=True)

            def couple(n, odd, x_load=None):
                for h in range(2):
                    pe.wait_ge(th_hi[h], n + 1)
                    for j in range(J):
                        for k in range(h * HJ, (h + 1) * HJ):
                            block_products(odd, j, k, w_lo, 1, 0, start=(j % HJ == 0 and k == 0))
                for h in range(2):
                    pe.wait_ge(th_lo[h], n + 1)
                    for jh in range(2):
                        if jh == 1 and h == 0 and x_load is not None:
                            pe.wait_ge(x_in, 16 * (x_load + 1))
                        for j in range(jh * HJ, (jh + 1) * HJ):
                            for k in range(h * HJ, (h + 1) * HJ):
                                last = block_products(odd, j, k, w_hi, slice(0, 2), slice(0, 2), stop=(k == J - 1))
                        if h == 1:
                            last.then_inc(coupled[jh], 1)

            def chunk(i, first, last):
                for s in range(CH):
                    for k in range(K):
                        if s == CH - 1 and k == 1 and not last:
                            couple(SG * i + K * s + k, k % 2, x_load=i + 1)
                        else:
                            couple(SG * i + K * s + k, k % 2)
                        if s == 0 and k == 2 and not first:
                            turn_y(i - 1)
                        if s == CH - 1 and k == 1 and not last:
                            turn_x(i + 1)

            over_chunks(pe, chunk)
            turn_y(NCH - 1)

        @block.scalar
        def _(act):
            act.preload_act_table(ACT.Tanh)
            act.wait_ge(scales_ready, 1)
            scale_regs = []
            for m in range(4):
                reg = act.alloc_register(f"scale{m}")
                act.reg_load(reg, scales[0:1, m:m + 1].bitcast(u32))
                scale_regs.append(reg)
            one_over_s, s_h = scale_regs[0], scale_regs[1:]

            def take_x(step, s):
                src = x_ps[:, s:F * CH:CH]
                act.copy(x_t[:, s, :], src)
                for m in range(3):
                    last = act.activation(x3[:, m, :], src, ACT.Copy, scale=s_h[m])
                last.then_inc(x_next, 1)

            act.wait_ge(x_turned, 1)
            take_x(0, 0)

            def tanh_parts(n, k, step):
                for h in range(2):
                    act.wait_ge(q_ready[h], n + 1)
                    act.activation(t_hilo[:, h * HJ:(h + 1) * HJ, 0, :], half(q_in[:, k, :], h), ACT.Tanh,
                                   scale=one_over_s).then_inc(th_hi[h], 1)
                    act.activation(t_full[:, h * HF:(h + 1) * HF], q_in[:, k, h * HF:(h + 1) * HF], ACT.Tanh,
                                   scale=one_over_s).then_inc(th_full[h], 1)
                if k == 0:
                    act.wait_ge(q_clipped, step + 1)
                act.activation(q_sq[:, :], q0[:, :] if k == 0 else q_in[:, k, :], ACT.Square,
                               scale=one_over_s).then_inc(sq_ready, 1)
                if k == 0:
                    act.activation(q_true[:, :], q0[:, :], ACT.Copy, scale=one_over_s).then_inc(q_unscaled, 1)

            def chunk(i, first, last):
                for s in range(CH):
                    for k in range(K):
                        step = CH * i + s
                        tanh_parts(SG * i + K * s + k, k, step)
                        if k == 2 and not (last and s == CH - 1):
                            act.wait_ge(drive_ready, step + 1)
                            if s == CH - 1:
                                act.wait_ge(x_turned, i + 2)
                            take_x(step + 1, (s + 1) % CH)
                        if s == 0 and k == 3 and not first:
                            take_y(i - 1)

            def take_y(c):
                act.wait_ge(y_turned, c + 1)
                act.copy(y_nat[:, :, :], y_ps[:, :, :]).then_inc(y_out_ready, 1)

            over_chunks(act, chunk)
            act.wait_ge(y_stored, 16 * JJ * (NCH - 1))
            act.wait_ge(q_clipped, T + 1)
            act.activation(q_true[:, :], q0[:, :], ACT.Copy, scale=one_over_s).then_inc(q_unscaled, 1)
            take_y(NCH - 1)

        LINKS = 8

        @block.gpsimd
        def _(pool):
            nc.gpsimd.memset(ident[:, :], 0.0).then_inc(ident_zeroed, 1)
            pool.wait_ge(ident_zeroed, 1)
            nc.gpsimd.affine_select(out=ident[:, :], in_=ident[:, :], compare_op=ALU.not_equal, fill=1.0, base=0,
                                    pattern=[[-1, P]], channel_multiplier=1).then_inc(ident_ready, 1)
            pool.wait_ge(top_of_rows, 1)
            nc.gpsimd.partition_all_reduce(c_top[:, 3:4], c_top[:, 2:3], P,
                                           bass.bass_isa.ReduceOp.max).then_inc(top_of_all, 1)
            pool.wait_ge(bias_ready, 1)

            def add_bias(step):
                pool.wait_ge(x_next, step + 1)
                pool.tensor_tensor(drive3[:, :, :], x3[:, :, :], bias3[:, :, :], ALU.add).then_inc(drive_ready, 1)

            add_bias(0)

            def finish_step(step, s):
                pool.wait_ge(q_unscaled, step + 2)
                pool.tensor_tensor(y_t[:, s:F * CH:CH], q_true[:, :], x_t[:, s, :], ALU.add).then_inc(y_done, 1)

            def chunk(i, first, last):
                for s in range(CH):
                    step = CH * i + s
                    n = SG * i + K * s
                    links = [0]

                    def link(ins):
                        links[0] += 1
                        ins.then_inc(sum_chain, 1)
                        return LINKS * step + links[0]

                    def add(dst, a, b):
                        return pool.tensor_tensor(dst, a, b, ALU.add)

                    def less(dst, a, b):
                        return pool.tensor_tensor(dst, a, b, ALU.subtract)

                    pool.wait_ge(p_clipped, step + 1)
                    add(p_off[:, :, :], p_in[:, 0, :].unsqueeze(1).broadcast_to([P, 2, F]),
                        alpha3[:, 0:2, :]).then_inc(p_off_ready, 1)
                    pool.wait_ge(q_clipped, step + 1)
                    pool.wait_ge(drive_ready, step + 1)
                    add(q_drive[:, :, :], drive3[:, 0:2, :],
                        q0[:, :].unsqueeze(1).broadcast_to([P, 2, F])).then_inc(q_drive_ready, 1)
                    pool.wait_ge(leak_ready, n + 1)
                    link(add(leak_sum[:, 0, :], leak[:, 0, :], alpha3[:, 2, :]))
                    if not (first and s == 0):
                        finish_step(step - 1, (s - 1) % CH)
                    pool.wait_ge(q_ready[1], n + 2)
                    moved = link(less(dq[:, :], q_in[:, 1, :], q0[:, :]))
                    pool.wait_ge(sum_chain, moved)
                    third = link(pool.tensor_tensor(dq_third[:, :], dq[:, :], thirds[:, :], ALU.mult))
                    pool.wait_ge(sum_chain, third)
                    add(q_middle[:, :], dq_third[:, :], drive3[:, 2, :]).then_inc(q_middle_ready, 1)
                    pool.wait_ge(leak_ready, n + 2)
                    twice = link(add(leak_twice[:, 0, :], leak[:, 1, :], leak[:, 1, :]))
                    pool.wait_ge(sum_chain, twice)
                    link(add(leak_sum[:, 1, :], leak_twice[:, 0, :], leak_sum[:, 0, :]))
                    pool.wait_ge(leak_ready, n + 3)
                    twice = link(add(leak_twice[:, 1, :], leak[:, 2, :], leak[:, 2, :]))
                    pool.wait_ge(sum_chain, twice)
                    summed = link(add(leak_sum[:, 2, :], leak_twice[:, 1, :], leak_sum[:, 1, :]))
                    pool.wait_ge(sum_chain, summed)
                    scaled = link(pool.tensor_tensor(p_moved[:, :], leak_sum[:, 2, :], p_gain[:, :], ALU.mult))
                    pool.wait_ge(sum_chain, scaled)
                    add(p_most[:, :], p_moved[:, :], p_in[:, 0, :]).then_inc(p_most_ready, 1)
                    if not (last and s == CH - 1):
                        add_bias(step + 1)
                        pool.wait_ge(p_summed, step + 1)
                        add(pool_spare[:, s:s + 1], bounds[:, 0:1], bounds[:, 1:2])
                        pool.tensor_scalar(p_in[:, 0, :], p_new[:, :], bounds[:, 0:1], bounds[:, 1:2], ALU.min,
                                           ALU.max).then_inc(p_clipped, 1)
                    assert links[0] == LINKS

            over_chunks(pool, chunk)
            finish_step(T - 1, CH - 1)

        @block.vector
        def _(dve):
            links = [0]

            def link(ins):
                links[0] += 1
                ins.then_inc(setup_chain, 1)
                dve.wait_ge(setup_chain, links[0])

            dve.wait_ge(coupling_in, 16)
            link(dve.tensor_reduce(c_top[:, 0:1], c_nat[:, :, :], AX.XY, ALU.max))
            link(dve.tensor_reduce(c_top[:, 1:2], c_nat[:, :, :], AX.XY, ALU.min))
            dve.scalar_tensor_tensor(c_top[:, 2:3], c_top[:, 1:2], -1.0, c_top[:, 0:1], ALU.mult,
                                     ALU.max).then_inc(top_of_rows, 1)
            dve.wait_ge(top_of_all, 1)
            link(dve.tensor_scalar(inv_s[:, :], c_top[:, 3:4], H3[0], 2.0 ** -60, ALU.mult, ALU.max))
            link(dve.tensor_scalar(s_up[:, :].bitcast(u32), inv_s[:, :].bitcast(u32), 0x7F800000, None,
                                   ALU.bitwise_and))
            link(dve.tensor_scalar(inv_s[:, :], s_up[:, :], 2.0 ** -14, None, ALU.mult))
            link(dve.reciprocal(s_up[:, :], inv_s[:, :]))
            for m in range(3):
                link(dve.tensor_scalar(scales[:, 1 + m:2 + m], s_up[:, :], H3[m], None, ALU.mult))
            link(dve.tensor_scalar(bounds[:, 0:1], s_up[:, :], CLAMP, None, ALU.mult))
            link(dve.tensor_scalar(bounds[:, 1:2], s_up[:, :], -CLAMP, None, ALU.mult))
            dve.tensor_copy(scales[:, 0:1], inv_s[:, :]).then_inc(scales_ready, 1)
            dve.wait_ge(setup_turned, 1)
            for m in range(3):
                bias_cols = setup_ps[:, F:F + J].unsqueeze(2).broadcast_to([P, J, B])
                link(dve.tensor_scalar(bias3[:, m, :].rearrange("p (j b) -> p j b", j=J), bias_cols,
                                       scales[:, 1 + m:2 + m], None, ALU.mult))
            for m, a in enumerate((H3[0] * EPSILON * ALPHA, H3[1] * EPSILON * ALPHA, 6 * ALPHA)):
                link(dve.memset(part[:, :], a))
                link(dve.tensor_scalar(alpha3[:, m, :], part[:, :], s_up[:, 0:1], None, ALU.mult))
            link(dve.memset(thirds[:, :], 1.0 / 3.0))
            link(dve.memset(p_gain[:, :], DT * EPSILON / 6.0))
            dve.tensor_scalar(p_in[:, 0, :], setup_ps[:, 0:F], s_up[:, 0:1], None, ALU.mult).then_inc(p_clipped, 1)
            dve.tensor_scalar(q_in[:, 0, :], setup_ps[:, 0:F], s_up[:, 0:1], None, ALU.mult).then_inc(bias_ready, 1)
            for k in range(J):
                dve.wait_ge(weights_turned, k + 1)
                link(dve.tensor_scalar(w_scaled[:, :], wt_ps[k % 2][:, :], H3[0], s_up[:, 0:1], ALU.mult, ALU.mult))
                link(dve.tensor_copy(w_hi[:, k, :], w_scaled[:, :]))
                link(dve.scalar_tensor_tensor(w_rest[:, :], w_hi[:, k, :], -1.0, w_scaled[:, :], ALU.mult, ALU.add))
                dve.tensor_scalar(w_lo[:, k, :], w_rest[:, :], LO, None, ALU.mult).then_inc(weights_taken, 1)
                dve.wait_ge(weights_taken, k + 1)
            for h in range(2):
                dve.sem_inc(q_ready[h], 1)

            spares = [0]

            def clip_q(n):
                dve.wait_ge(q_ready[1], n + 1)
                dve.tensor_scalar(q0[:, :], q_in[:, 0, :], bounds[:, 0:1], bounds[:, 1:2], ALU.min,
                                  ALU.max).then_inc(q_clipped, 1)

            def split_tanh(n, h):
                carry(th_full[h], n)
                dve.tensor_tensor_reduce(t_hilo[:, h * HJ:(h + 1) * HJ, 1, :], half(t_full, h),
                                         t_hilo[:, h * HJ:(h + 1) * HJ, 0, :], LO, 0.0, ALU.subtract, ALU.max,
                                         t_lo_top[:, h:h + 1]).then_inc(th_lo[h], 1)

            def take_leak(k, q):
                dve.scalar_tensor_tensor(leak[:, k, :], p_in[:, k, :], -BETA, q, ALU.mult,
                                         ALU.add).then_inc(leak_ready, 1)

            def next_p(k):
                ins = dve.scalar_tensor_tensor(p_in[:, k + 1, :], leak[:, k, :], H3[H_OF[k]] * EPSILON,
                                               p_off[:, H_OF[k], :], ALU.mult, ALU.add)
                if k == 0:
                    ins.then_inc(p1_ready, 1)

            def less_p(k):
                on = q_last[:, :] if k == 3 else q_drive[:, H_OF[k], :]
                ins = dve.scalar_tensor_tensor(base[:, k, :], p_in[:, k, :], -H3[H_OF[k]], on, ALU.mult, ALU.add)
                if k == K - 1:
                    ins.then_inc(base_ready, 1)

            def carry(semaphore, n):
                dve.wait_ge(semaphore, n + 1)
                spares[0] = (spares[0] + 1) % SPARES
                dve.memset(spare[:, spares[0]:spares[0] + 1], 0.0)

            def take_cubic(n, q):
                dve.wait_ge(sq_ready, n + 1)
                dve.scalar_tensor_tensor(cubic[:, :], q_sq[:, :], -3.0, q, ALU.add, ALU.mult).then_inc(cubic_ready, 1)

            def take_pre(k, base_k):
                for h in range(2):
                    cols = slice(h * HF, (h + 1) * HF)
                    dve.scalar_tensor_tensor(pre[:, k, cols], cubic[:, cols], -H3[H_OF[k]] / 3.0, base_k[:, cols],
                                             ALU.mult, ALU.add).then_inc(pre_ready[h], 1)

            def ahead(n, k, step, at_end=False):
                if k == 0:
                    dve.wait_ge(p_clipped, step + 1)
                    dve.scalar_tensor_tensor(slope0[:, :], p_in[:, 0, :], -H3[0], drive3[:, 0, :], ALU.mult,
                                             ALU.add)
                    clip_q(n)
                    split_tanh(n, 0)
                    dve.wait_ge(q_clipped, step + 1)
                    dve.tensor_tensor(base[:, 0, :], slope0[:, :], q0[:, :], ALU.add)
                    split_tanh(n, 1)
                    take_cubic(n, q0[:, :])
                    dve.wait_ge(p_off_ready, step + 1)
                    take_leak(k, q0[:, :])
                    dve.wait_ge(cubic_ready, n + 1)
                    take_pre(k, base[:, k])
                    carry(q_drive_ready, step)
                elif k == 1:
                    dve.wait_ge(leak_ready, n)
                    next_p(0)
                    carry(q_ready[1], n)
                    dve.wait_ge(p1_ready, step + 1)
                    less_p(k)
                    split_tanh(n, 0)
                    take_leak(k, q_in[:, k, :])
                    split_tanh(n, 1)
                    take_cubic(n, q_in[:, k, :])
                    dve.wait_ge(leak_ready, n + 1)
                    next_p(k)
                    dve.wait_ge(cubic_ready, n + 1)
                    take_pre(k, base[:, k])
                elif k == 2:
                    less_p(k)
                    dve.wait_ge(q_ready[1], n + 1)
                    take_leak(k, q_in[:, k, :])
                    dve.wait_ge(q_middle_ready, step + 1)
                    dve.scalar_tensor_tensor(q_last[:, :], q_in[:, 2, :], TWO_THIRDS, q_middle[:, :], ALU.mult,
                                             ALU.add).then_inc(q_last_ready, 1)
                    split_tanh(n, 0)
                    split_tanh(n, 1)
                    take_cubic(n, q_in[:, k, :])
                    dve.wait_ge(leak_ready, n + 1)
                    next_p(k)
                    dve.wait_ge(cubic_ready, n + 1)
                    take_pre(k, base[:, k])
                else:
                    dve.wait_ge(q_last_ready, step + 1)
                    less_p(k)
                    dve.wait_ge(q_ready[1], n + 1)
                    take_leak(k, q_in[:, k, :])
                    dve.wait_ge(base_ready, step + 1)
                    dve.scalar_tensor_tensor(base_last[:, :], q_in[:, 3, :], ONE_THIRD, base[:, 3, :], ALU.mult,
                                             ALU.add)
                    carry(p_most_ready, step)
                    split_tanh(n, 0)
                    dve.wait_ge(leak_ready, n + 1)
                    dve.scalar_tensor_tensor(p_new[:, :], leak[:, 3, :], DT * EPSILON / 6.0, p_most[:, :],
                                             ALU.mult, ALU.add).then_inc(p_summed, 1)
                    split_tanh(n, 1)
                    take_cubic(n, q_in[:, k, :])
                    if not at_end:
                        carry(drive_ready, step + 1)
                    dve.wait_ge(cubic_ready, n + 1)
                    take_pre(k, base_last)

            def close(n, k):
                for h in range(2):
                    carry(pre_ready[h], n)
                    dve.wait_ge(coupled[h], n + 1)
                    dve.scalar_tensor_tensor(half(part, h), g_ps[k % 2][h][:, :, 1, :], G_TIMES[k] / LO,
                                             half(pre[:, k, :], h), ALU.mult, ALU.add).then_inc(part_ready[h], 1)
                for h in range(2):
                    dve.wait_ge(part_ready[h], n + 1)
                    dve.scalar_tensor_tensor(half(q_in[:, (k + 1) % K, :], h), g_ps[k % 2][h][:, :, 0, :], G_TIMES[k],
                                             half(part, h), ALU.mult, ALU.add).then_inc(q_ready[h], 1)

            carry(drive_ready, 0)
            ahead(0, 0, 0)

            def chunk(i, first, last):
                for s in range(CH):
                    for k in range(K):
                        n = SG * i + K * s + k
                        step = CH * i + s
                        close(n, k)
                        if k < K - 1:
                            ahead(n + 1, k + 1, step, at_end=last and s == CH - 1)
                        elif not (last and s == CH - 1):
                            ahead(n + 1, 0, step + 1)

            over_chunks(dve, chunk)
            clip_q(K * T)


_INS = ["x", "cond_2048", "L0_cond_coupling", "L0_cond_bias"]


def kernel(**inputs):
    import numpy as _np
    import concourse.bacc as _bacc
    from concourse import mybir as _mybir
    from concourse.bass_utils import run_bass_kernel_spmd as _run

    nc = _bacc.Bacc("TRN2", target_bir_lowering=False, num_devices=1)
    arrays, args = {}, []
    for name in _INS:
        a = _np.ascontiguousarray(inputs[name])
        arrays[f"in_{name}"] = a
        args.append(nc.dram_tensor(f"in_{name}", a.shape, _mybir.dt.from_np(a.dtype), kind="ExternalInput").ap())
    shape = tuple(inputs["x"].shape)
    args.append(nc.dram_tensor("out_0", shape, _mybir.dt.float32, kind="ExternalOutput").ap())
    build(nc, *args)
    r = _run(nc, [arrays], core_ids=[0])
    return r.results[0]["out_0"]
```
